# Optimizing a Trainium2 kernel written in Bass

```python
import numpy as np
import jax
import jax.numpy as jnp

def _softmax(x, axis=-1):
    return jax.nn.softmax(x, axis=axis)

def _gelu(x):
    return jax.nn.gelu(x, approximate=True)

def _silu(x):
    return jax.nn.silu(x)

def _sigmoid(x):
    return jax.nn.sigmoid(x)

def _layernorm(x, axis=-1, eps=1e-05):
    m = jnp.mean(x, axis=axis, keepdims=True)
    v = jnp.var(x, axis=axis, keepdims=True)
    return (x - m) / jnp.sqrt(v + eps)

def _scatter_add(tgt, idx, src, axis=0):
    return tgt.at[idx].add(src)

def _segment_sum(src, seg, n):
    return jax.ops.segment_sum(src, seg, n)
kernel_name = 'mk_cond_resid_d4_seqx_r2_f6d737'

def setup_inputs(seed: int=0):
    np.random.seed(seed)
    _w = jnp.asarray

    def _rec_inputs():
        import jax
        import jax.numpy as jnp
        _rk = jax.random.key(seed)
        x = 4.136e-05 + 0.9999 * jax.random.normal(jax.random.fold_in(_rk, 1), (8, 512, 512), jnp.float32)
        _lenS = 512 - jax.random.randint(jax.random.fold_in(_rk, 7), (8,), 0, max(1, 512 // 4) + 1, jnp.int32)
        _lenS2 = 512 - jax.random.randint(jax.random.fold_in(_rk, 8), (8,), 0, max(1, 512 // 4) + 1, jnp.int32)
        cond_1024 = -0.00608245 + 1.00131 * jax.random.normal(jax.random.fold_in(_rk, 11), (8, 512), jnp.float32)
        return (x, cond_1024)
    x, cond_1024 = _rec_inputs()

    def _L0_cond_setup():
        import jax, jax.numpy as jnp
        import numpy as np
        B, T, D_IN, V_IN, E = (64, 128, 512, 512, 512)
        key = jax.random.key(seed)
        ks = jax.random.split(key, 16)
        s = 0.01
        return {'video': jax.random.normal(ks[0], (B, V_IN), jnp.float32), 'seq': jax.random.normal(ks[1], (B, T, D_IN), jnp.float32), 'W_z': jax.random.normal(ks[2], (D_IN, E), jnp.float32) * s, 'U_z': jax.random.normal(ks[3], (E, E), jnp.float32) * s, 'C_z': jax.random.normal(ks[4], (V_IN, E), jnp.float32) * s, 'b_z': jnp.zeros((E,), jnp.float32), 'W_r': jax.random.normal(ks[5], (D_IN, E), jnp.float32) * s, 'U_r': jax.random.normal(ks[6], (E, E), jnp.float32) * s, 'C_r': jax.random.normal(ks[7], (V_IN, E), jnp.float32) * s, 'b_r': jnp.zeros((E,), jnp.float32), 'W': jax.random.normal(ks[8], (D_IN, E), jnp.float32) * s, 'U': jax.random.normal(ks[9], (E, E), jnp.float32) * s, 'C': jax.random.normal(ks[10], (V_IN, E), jnp.float32) * s, 'b': jnp.zeros((E,), jnp.float32)}
    _L0_cond_all = _L0_cond_setup()
    _L0_cond_in = {k: v for k, v in _L0_cond_all.items() if k in ('W_z', 'U_z', 'C_z', 'b_z', 'W_r', 'U_r', 'C_r', 'b_r', 'W', 'U', 'C', 'b')}
    del _L0_cond_all

    def _L1_cond_setup():
        import jax, jax.numpy as jnp
        import numpy as np
        key = jax.random.key(seed)
        ks = jax.random.split(key, 8)
        B, L, D, N, K = (4, 2048, 512, 64, 4)
        return {'x': jax.random.normal(ks[0], (B, L, D), dtype=jnp.float32), 'conv_w': jax.random.normal(ks[1], (K, 1, D), dtype=jnp.float32) * 0.1, 'conv_b': jnp.zeros((D,), dtype=jnp.float32), 'Wp': jax.random.normal(ks[2], (D, 2 * N), dtype=jnp.float32) * (1.0 / np.sqrt(D)), 'bp': jnp.zeros((2 * N,), dtype=jnp.float32), 'Ws': jax.random.normal(ks[3], (D, N), dtype=jnp.float32) * (1.0 / np.sqrt(D)), 'bs': jnp.zeros((N,), dtype=jnp.float32), 'A_log': jax.random.normal(ks[4], (N,), dtype=jnp.float32) * 0.02, 'dt_log': jax.random.normal(ks[5], (N,), dtype=jnp.float32) * 0.02, 'Wo': jax.random.normal(ks[6], (N, D), dtype=jnp.float32) * (1.0 / np.sqrt(N)), 'bo': jnp.zeros((D,), dtype=jnp.float32)}
    _L1_cond_all = _L1_cond_setup()
    _L1_cond_in = {k: v for k, v in _L1_cond_all.items() if k in ('conv_b', 'Wp', 'bp', 'Ws', 'bs', 'A_log', 'dt_log', 'Wo', 'bo')}
    del _L1_cond_all

    def _L2_cond_setup():
        import jax, jax.numpy as jnp
        import numpy as np
        LATENT = 512
        key = jax.random.key(seed)
        k1, k2, k3, k4 = jax.random.split(key, 4)
        B, T, D = (64, 256, LATENT)
        h_t = jax.random.normal(k1, (B, D), dtype=jnp.float32)
        z = jax.random.normal(k2, (B, T, D), dtype=jnp.float32)
        bound = 1.0 / np.sqrt(2 * D)
        W = jax.random.uniform(k3, (D, 2 * D), minval=-bound, maxval=bound, dtype=jnp.float32)
        b = jax.random.uniform(k4, (D,), minval=-bound, maxval=bound, dtype=jnp.float32)
        alpha = jnp.full((D,), 0.1, dtype=jnp.float32)
        return {'h_t': h_t, 'z': z, 'W': W, 'b': b, 'alpha': alpha}
    _L2_cond_all = _L2_cond_setup()
    _L2_cond_in = {k: v for k, v in _L2_cond_all.items() if k in ('W', 'b', 'alpha')}
    del _L2_cond_all

    def _L3_cond_setup():
        import jax, jax.numpy as jnp
        import numpy as np
        RANK = 8
        LN_EPS = 1e-05
        key = jax.random.key(seed)
        ks = jax.random.split(key, 8)
        B, T, D = (16, 512, 512)
        A = 512
        I = 512
        OUT = D * RANK * 4
        s = 0.02
        return {'x': jax.random.normal(ks[0], (B, T, D), jnp.float32), 'ada_emb': jax.random.normal(ks[1], (B, A), jnp.float32), 'base_up': jax.random.normal(ks[2], (D, D), jnp.float32) * s, 'base_down': jax.random.normal(ks[3], (D, D), jnp.float32) * s, 'ln_gamma': jnp.ones((A,), jnp.float32), 'ln_beta': jnp.zeros((A,), jnp.float32), 'W1': jax.random.normal(ks[4], (A, I), jnp.float32) / np.sqrt(A), 'bias1': jnp.zeros((I,), jnp.float32), 'W2': jax.random.normal(ks[5], (I, OUT), jnp.float32) / np.sqrt(I), 'bias2': jnp.zeros((OUT,), jnp.float32)}
    _L3_cond_all = _L3_cond_setup()
    _L3_cond_in = {k: v for k, v in _L3_cond_all.items() if k in ('base_up', 'base_down', 'ln_gamma', 'ln_beta', 'W1', 'bias1', 'W2', 'bias2')}
    del _L3_cond_all
    return {'x': x, 'cond_1024': cond_1024, 'L0_cond_W_z': _L0_cond_in['W_z'], 'L0_cond_U_z': _L0_cond_in['U_z'], 'L0_cond_C_z': _L0_cond_in['C_z'], 'L0_cond_b_z': _L0_cond_in['b_z'], 'L0_cond_W_r': _L0_cond_in['W_r'], 'L0_cond_U_r': _L0_cond_in['U_r'], 'L0_cond_C_r': _L0_cond_in['C_r'], 'L0_cond_b_r': _L0_cond_in['b_r'], 'L0_cond_W': _L0_cond_in['W'], 'L0_cond_U': _L0_cond_in['U'], 'L0_cond_C': _L0_cond_in['C'], 'L0_cond_b': _L0_cond_in['b'], 'L1_cond_conv_b': _L1_cond_in['conv_b'], 'L1_cond_Wp': _L1_cond_in['Wp'], 'L1_cond_bp': _L1_cond_in['bp'], 'L1_cond_Ws': _L1_cond_in['Ws'], 'L1_cond_bs': _L1_cond_in['bs'], 'L1_cond_A_log': _L1_cond_in['A_log'], 'L1_cond_dt_log': _L1_cond_in['dt_log'], 'L1_cond_Wo': _L1_cond_in['Wo'], 'L1_cond_bo': _L1_cond_in['bo'], 'L2_cond_W': _L2_cond_in['W'], 'L2_cond_b': _L2_cond_in['b'], 'L2_cond_alpha': _L2_cond_in['alpha'], 'L3_cond_base_up': _L3_cond_in['base_up'], 'L3_cond_base_down': _L3_cond_in['base_down'], 'L3_cond_ln_gamma': _L3_cond_in['ln_gamma'], 'L3_cond_ln_beta': _L3_cond_in['ln_beta'], 'L3_cond_W1': _L3_cond_in['W1'], 'L3_cond_bias1': _L3_cond_in['bias1'], 'L3_cond_W2': _L3_cond_in['W2'], 'L3_cond_bias2': _L3_cond_in['bias2']}

def reference(x, cond_1024, L0_cond_W_z, L0_cond_U_z, L0_cond_C_z, L0_cond_b_z, L0_cond_W_r, L0_cond_U_r, L0_cond_C_r, L0_cond_b_r, L0_cond_W, L0_cond_U, L0_cond_C, L0_cond_b, L1_cond_conv_b, L1_cond_Wp, L1_cond_bp, L1_cond_Ws, L1_cond_bs, L1_cond_A_log, L1_cond_dt_log, L1_cond_Wo, L1_cond_bo, L2_cond_W, L2_cond_b, L2_cond_alpha, L3_cond_base_up, L3_cond_base_down, L3_cond_ln_gamma, L3_cond_ln_beta, L3_cond_W1, L3_cond_bias1, L3_cond_W2, L3_cond_bias2):
    import jax
    import jax.numpy as jnp

    def _L0_cond_ref(video, seq, W_z, U_z, C_z, b_z, W_r, U_r, C_r, b_r, W, U, C, b):
        import jax, jax.numpy as jnp
        import numpy as np
        B, T, D_IN, V_IN, E = (64, 128, 512, 512, 512)
        vz = video @ C_z + b_z
        vr = video @ C_r + b_r
        vh = video @ C + b
        xz = jnp.einsum('btd,de->bte', seq, W_z)
        xr = jnp.einsum('btd,de->bte', seq, W_r)
        xh = jnp.einsum('btd,de->bte', seq, W)

        def step(h, xs):
            xzt, xrt, xht = xs
            z = jax.nn.sigmoid(xzt + h @ U_z + vz)
            r = jax.nn.sigmoid(xrt + h @ U_r + vr)
            hh = jnp.tanh(xht + r * h @ U + vh)
            h_new = (1.0 - z) * h + z * hh
            return (h_new, h_new)
        h0 = jnp.zeros((seq.shape[0], U.shape[0]), seq.dtype)
        xs = (jnp.swapaxes(xz, 0, 1), jnp.swapaxes(xr, 0, 1), jnp.swapaxes(xh, 0, 1))
        _, out_t = jax.lax.scan(step, h0, xs)
        return jnp.swapaxes(out_t, 0, 1)

    def _L1_cond_ref(x, conv_w, conv_b, Wp, bp, Ws, bs, A_log, dt_log, Wo, bo):
        import jax, jax.numpy as jnp
        import numpy as np
        B, L, D = x.shape
        K = conv_w.shape[0]
        N = Ws.shape[1]
        x_pad = jnp.pad(x, ((0, 0), (K - 1, 0), (0, 0)))
        conv = conv_b + sum((x_pad[:, k:k + L, :] * conv_w[k, 0] for k in range(K)))
        proj = conv @ Wp + bp
        B_t = jax.nn.softplus(proj[..., :N])
        C_t = jnp.tanh(proj[..., N:])
        u = x @ Ws + bs
        A = -jax.nn.softplus(A_log)
        dt = jax.nn.softplus(dt_log)
        decay = 1.0 + dt * A

        def step(state, inputs):
            u_t, b_t, c_t = inputs
            state = decay * state + dt * b_t * u_t
            return (state, c_t * state)
        init = jnp.zeros((B, N), dtype=x.dtype)
        xs = tuple((jnp.swapaxes(a, 0, 1) for a in (u, B_t, C_t)))
        _, ys = jax.lax.scan(step, init, xs, unroll=4)
        y = jnp.swapaxes(ys, 0, 1)
        return y @ Wo + bo

    def _L2_cond_ref(h_t, z, W, b, alpha):
        import jax, jax.numpy as jnp
        import numpy as np
        LATENT = 512
        D = h_t.shape[-1]
        Wh = W[:, :D]
        Wz = W[:, D:]
        leak = 1.0 - alpha

        def step(h, z_t):
            gate = jax.nn.sigmoid(h @ Wh.T + z_t @ Wz.T + b)
            h_new = jnp.tanh(h * leak + gate * z_t)
            return (h_new, h_new)
        _, hs = jax.lax.scan(step, h_t, jnp.swapaxes(z, 0, 1))
        return jnp.swapaxes(hs, 0, 1)

    def _L3_cond_ref(x, ada_emb, base_up, base_down, ln_gamma, ln_beta, W1, bias1, W2, bias2):
        import jax, jax.numpy as jnp
        import numpy as np
        RANK = 8
        LN_EPS = 1e-05
        B, T, D = x.shape
        R = RANK
        mu = jnp.mean(ada_emb, axis=-1, keepdims=True)
        var = jnp.mean(jnp.square(ada_emb - mu), axis=-1, keepdims=True)
        c = (ada_emb - mu) / jnp.sqrt(var + LN_EPS) * ln_gamma + ln_beta
        h = jax.nn.gelu(c @ W1 + bias1, approximate=False)
        w = h @ W2 + bias2
        a1, b1, a2, b2 = [t.reshape(B, D, R) for t in jnp.split(w, 4, axis=-1)]
        u = jnp.einsum('btd,bdr->btr', x, a2)
        mid = jnp.einsum('btd,dl->btl', x, base_down) + jnp.einsum('btr,blr->btl', u, b2)
        mid = jax.nn.gelu(mid, approximate=False)
        v = jnp.einsum('blr,btl->btr', b1, mid)
        out = jnp.einsum('btl,kl->btk', mid, base_up) + jnp.einsum('bkr,btr->btk', a1, v)
        return x + out
    x = x + _L0_cond_ref(cond_1024, x, L0_cond_W_z, L0_cond_U_z, L0_cond_C_z, L0_cond_b_z, L0_cond_W_r, L0_cond_U_r, L0_cond_C_r, L0_cond_b_r, L0_cond_W, L0_cond_U, L0_cond_C, L0_cond_b)
    x = x + _L1_cond_ref(x, cond_1024[:, None, :], L1_cond_conv_b, L1_cond_Wp, L1_cond_bp, L1_cond_Ws, L1_cond_bs, L1_cond_A_log, L1_cond_dt_log, L1_cond_Wo, L1_cond_bo)
    x = x + _L2_cond_ref(cond_1024, x, L2_cond_W, L2_cond_b, L2_cond_alpha)
    x = x + _L3_cond_ref(x, cond_1024, L3_cond_base_up, L3_cond_base_down, L3_cond_ln_gamma, L3_cond_ln_beta, L3_cond_W1, L3_cond_bias1, L3_cond_W2, L3_cond_bias2)
    return x

_drawn_inputs = setup_inputs


def setup_inputs(seed=0):
    import zlib

    import numpy as np

    out = dict(_drawn_inputs(seed))
    spreads = {'L0_cond_b_z': (0.0, 0.8),
     'L0_cond_b_r': (0.0, 2.0),
     'L0_cond_b': (0.0, 0.1),
     'L1_cond_conv_b': (0.0, 0.1),
     'L1_cond_bp': (0.0, 0.1),
     'L1_cond_bs': (0.0, 0.1),
     'L1_cond_bo': (0.0, 0.1),
     'L2_cond_alpha': (0.10000000149011612, 0.6),
     'L3_cond_ln_gamma': (1.0, 0.2),
     'L3_cond_ln_beta': (0.0, 0.1),
     'L3_cond_bias1': (0.0, 0.1),
     'L3_cond_bias2': (0.0, 0.1)}
    factors = {'L0_cond_U_z': 8.0,
     'L0_cond_C_z': 2.82,
     'L0_cond_W_r': 32.289,
     'L0_cond_U_r': 200.0,
     'L0_cond_C_r': 43.074,
     'L1_cond_A_log': 6.424,
     'L1_cond_dt_log': 4.698,
     'L2_cond_b': 41.971,
     'L3_cond_base_up': 3.816,
     'L3_cond_base_down': 3.698}
    for name, (base, spread) in spreads.items():
        noise = np.random.default_rng([zlib.crc32(name.encode()), seed]).standard_normal(out[name].shape)
        drawn = base * np.exp(spread * noise) if base else spread * noise
        out[name] = jnp.asarray(drawn.astype(out[name].dtype))
    for name, factor in factors.items():
        out[name] = (out[name] * factor).astype(out[name].dtype)
    return out
```

```python
import concourse.bass as bass
from concourse import mybir
from contextlib import ExitStack


B, T, E, P = 8, 512, 512, 128
KT = E // P
STEPS = 16
TOK = STEPS * B
CHUNKS = T // STEPS
TAPS = B
HIST = (TAPS - 1) * B
N1 = 64
RANK = 8
LR = RANK * B
PIECES = 4 * RANK
SLOTS = 4
PARTS = 3
GR, GZ, GH, GG = range(4)
(V_BZ, V_BR, V_B, V_CONVB, V_BO, V_L2B, V_ALPHA, V_GAMMA, V_BETA, V_BIAS1) = range(10)
V_BIAS2 = 10 * KT
V_COND = V_BIAS2 + PIECES * KT
V_ALL = V_COND + KT * B
(S_BPB, S_BPC, S_BS, S_ALOG, S_DTLOG) = range(5)
LN_EPS = 1e-5
SERIES = 7
K_SOFT = 6 + SERIES
K_L1 = K_SOFT + 5
K_F = 2


def four_layer_kernel(nc, x_in, w_stage, w2_in, w_proj, vecs_in, cond_in, wp_in, ws_in, wo_in, small_in, out):
    fp32, bf16 = mybir.dt.float32, mybir.dt.bfloat16
    ALU, ACT, AX = mybir.AluOpType, mybir.ActivationFunctionType, mybir.AxisListType

    with ExitStack() as ctx:
        def sb(name, shape, dt=fp32):
            return ctx.enter_context(nc.sbuf_tensor(name, shape, dt))

        def bank(name):
            return ctx.enter_context(nc.psum_tensor(name, [P, 512], fp32))

        def sem(name):
            return ctx.enter_context(nc.semaphore(name))

        U = sb("U", [P, 4, PARTS, KT, E], bf16)
        PW = sb("PW", [P, 6, KT, E])
        W_R, W_Z, W_H, W_G, W_DOWN, W_UP = range(6)
        WP = sb("WP", [P, KT, 2 * N1])
        WS = sb("WS", [P, KT, N1])
        WO = sb("WO", [N1, E])
        stage = sb("stage", [P, SLOTS, KT, E])
        vecs = sb("vecs", [P, V_ALL])
        small = sb("small", [N1, 5])
        identf = sb("identf", [P, P])
        identb = sb("identb", [P, P], bf16)
        batchmask = sb("batchmask", [LR, B])
        vbias = sb("vbias", [P, 3, KT, B])
        leak = sb("leak", [P, KT])
        zeros = sb("zeros", [P, KT])
        dec_dt = sb("dec_dt", [N1, 2])
        decmask = sb("decmask", [N1, B, STEPS])
        sp2 = sb("sp2", [N1, 6, 2])
        lns = sb("lns", [B, 4])
        cT = sb("cT", [P, KT, B])
        cTg = sb("cTg", [P, KT, B])
        hpre = sb("hpre", [P, KT, B])
        hT = sb("hT", [P, KT, B])
        lowrank = sb("lowrank", [P, PIECES, KT, B])
        w2rows = sb("w2rows", [B, E])
        A2 = sb("A2", [P, KT, RANK, B])
        B1 = sb("B1", [P, KT, RANK, B])
        A1B2 = sb("A1B2", [P, 2, KT, RANK, B])
        A1T = sb("A1T", [LR, E])
        B2T = sb("B2T", [LR, E])
        HS = sb("HS", [P, PARTS, KT, B])
        RH = sb("RH", [P, PARTS, KT, B])
        HG = sb("HG", [P, PARTS, KT, B])
        SR, SZ, SH, SG = (sb(n, [P, KT, B]) for n in ("SR", "SZ", "SH", "SG"))
        RT, ZT, HT, GT = (sb(n, [P, KT, B]) for n in ("RT", "ZT", "HT", "GT"))
        ZC, ZH, HL, ZX, GX, GP = (sb(n, [P, KT, B]) for n in ("ZC", "ZH", "HL", "ZX", "GX", "GP"))
        X = sb("X", [P, 2, KT, TOK])
        X1 = sb("X1", [P, 2, KT, HIST + TOK])
        F = sb("F", [P, 4, PARTS, KT, TOK])
        CONV = sb("CONV", [P, KT, TOK])
        CM = sb("CM", [P, 2, TOK])
        X2 = sb("X2", [P, KT, TOK])
        X3 = sb("X3", [P, KT, TOK])
        MT = sb("MT", [P, KT, TOK])
        OUTB = sb("OUTB", [P, KT, TOK])
        cond, cn, lnsq = (t[0:B, :, :].rearrange("p k n -> p (k n)") for t in (X3, MT, OUTB))
        XB, AX1, RL, CL, US, CT, QS, DS, RD, SS, WW, AC, SP, YT = (
            sb(n, [N1, TOK]) for n in ("XB", "AX1", "RL", "CL", "US", "CT", "QS", "DS", "RD", "SS", "WW", "AC", "SP", "YT"))
        VV = sb("VV", [N1, B, STEPS])
        YS = sb("YS", [N1, B, STEPS])
        UM = sb("UM", [LR, TOK])
        VM = sb("VM", [LR, TOK])

        A = [bank("A0"), bank("A1")]
        Z, G = bank("Z"), bank("G")
        C0, C1, C2, C3 = (bank(f"C{i}") for i in range(4))

        ident_set = sem("ident_set")
        vecs_loaded = sem("vecs_loaded")
        small_loaded = sem("small_loaded")
        cond_loaded = sem("cond_loaded")
        l1w_in = sem("l1w_in")
        stored = sem("stored")
        idents = sem("idents")
        hi_done = sem("hi_done")
        rem_done = sem("rem_done")
        mid_done3 = sem("mid_done3")
        split_done = sem("split_done")
        cond_prod_done = sem("cond_prod_done")
        ln_var = sem("ln_var")
        ln_root = sem("ln_root")
        ln_ready = sem("ln_ready")
        ct_prod_done = sem("ct_prod_done")
        ct_ready = sem("ct_ready")
        h_prod_done = sem("h_prod_done")
        h_pre_ready = sem("h_pre_ready")
        ht_ready = sem("ht_ready")
        w2_done = sem("w2_done")
        w2_rows_copied = sem("w2_rows_copied")
        w2_turned = sem("w2_turned")
        lr_evac = sem("lr_evac")
        pro_chain = sem("pro_chain")
        lr_packed = sem("lr_packed")
        lrt_done = sem("lrt_done")
        lrt_evac = sem("lrt_evac")
        pro_abs = sem("pro_abs")
        pro_sig = sem("pro_sig")
        preR_done = [sem(f"preR_done{j}") for j in range(2)]
        preH_done = [sem(f"preH_done{j}") for j in range(2)]
        preZ_done = sem("preZ_done")
        preG_done = sem("preG_done")
        sumR_done = [sem(f"sumR_done{j}") for j in range(2)]
        sumH_done = [sem(f"sumH_done{j}") for j in range(2)]
        sumZ_done = sem("sumZ_done")
        sumG_done = sem("sumG_done")
        r_ready = [sem(f"r_ready{j}") for j in range(2)]
        z_ready = sem("z_ready")
        hh_ready = [sem(f"hh_ready{j}") for j in range(2)]
        gate_ready = sem("gate_ready")
        gp_ready = sem("gp_ready")
        hg_new = sem("hg_new")
        rh_ready = [sem(f"rh_ready{j}") for j in range(2)]
        h_ready = [sem(f"h_ready{j}") for j in range(2)]
        hg_ready = sem("hg_ready")
        x1_added = sem("x1_added")
        x3_added = sem("x3_added")
        conv_mul = sem("conv_mul")
        conv_added = sem("conv_added")
        x2_init = sem("x2_init")
        rh_new = [sem(f"rh_new{j}") for j in range(2)]
        rh_rem = [sem(f"rh_rem{j}") for j in range(2)]
        zc_done = sem("zc_done")
        zh_done = [sem(f"zh_done{j}") for j in range(2)]
        h_new = [sem(f"h_new{j}") for j in range(2)]
        h_rem = [sem(f"h_rem{j}") for j in range(2)]
        hl_done = sem("hl_done")
        zx_copied = sem("zx_copied")
        gx_done = sem("gx_done")
        hg_rem = sem("hg_rem")
        chain_l1 = sem("chain_l1")
        chain_f = sem("chain_f")
        chain_fg = sem("chain_fg")
        l1_proj_done = sem("l1_proj_done")
        l1_abs = sem("l1_abs")
        l1_c = sem("l1_c")
        l1_evac = sem("l1_evac")
        l1_sig = sem("l1_sig")
        l1_tanh = sem("l1_tanh")
        y_ready = sem("y_ready")
        lr_u_done = sem("lr_u_done")
        u_masked = sem("u_masked")
        projR_done = sem("projR_done")
        projZ_done = sem("projZ_done")
        projH_done = sem("projH_done")
        F_R = sem("F_R")
        F_Z = sem("F_Z")
        F_H = sem("F_H")
        projG_done = sem("projG_done")
        F_G = sem("F_G")
        mid_done = sem("mid_done")
        mid_act = sem("mid_act")
        wo_done = sem("wo_done")
        x2_ready = sem("x2_ready")
        v_done = sem("v_done")
        v_masked = sem("v_masked")
        out_done = sem("out_done")
        out_ready = sem("out_ready")
        hist_copied = sem("hist_copied")
        vb_ready = sem("vb_ready")
        piece_in = [sem(f"piece_in{n}") for n in range(SLOTS)]
        w_proj_in = [sem(f"w_proj_in{n}") for n in range(6)]
        x_loaded = [sem(f"x_loaded{n}") for n in range(2)]

        class Count:
            def __init__(self, base):
                self.base, self.n = base, 0

            def next(self):
                self.n += 1
                return self.base + self.n

        HSh = HS[:, :, :, :].bitcast(bf16).rearrange("p g k (b two) -> p g k b two", two=2)
        RHh = RH[:, :, :, :].bitcast(bf16).rearrange("p g k (b two) -> p g k b two", two=2)
        HGh = HG[:, :, :, :].bitcast(bf16).rearrange("p g k (b two) -> p g k b two", two=2)
        Fh = F[:, :, :, :, :].bitcast(bf16).rearrange("p a g m (n two) -> p a g m n two", two=2)

        def vec(i):
            return vecs[:, i * KT:(i + 1) * KT]

        condT = vecs[:, V_COND:V_COND + KT * B].rearrange("p (k b) -> p k b", b=B)

        HALVES = ((0, slice(0, 2)), (1, slice(2, 4)))

        def over_b(v):
            return v.unsqueeze(2).to_broadcast([P, KT, B])

        def over_tok(v, n=KT):
            return v.unsqueeze(2).to_broadcast([P, n, TOK])

        def mask_tok():
            return batchmask[:, :].unsqueeze(1).to_broadcast([LR, STEPS, B])

        def on(i, first, last):
            return not isinstance(i, int) or first <= i <= last

        def at(i, n):
            return isinstance(i, int) and i == n

        def l0_on(i): return on(i, 0, CHUNKS - 1)
        def conv_on(i): return on(i, 1, CHUNKS)
        def l2_on(i): return on(i, 2, CHUNKS + 1)
        def l3_on(i): return on(i, 3, CHUNKS + 2)
        def l0_chunks(i):
            return min(i + 1, CHUNKS) if isinstance(i, int) else i + 1

        def w2_on(i): return isinstance(i, int) and i < 2

        HEAD = 4
        LAST = CHUNKS + 2

        def wavefront(eng, iteration):
            for i in range(HEAD):
                iteration(i, i % 2)
            with eng.Fori(HEAD // 2, CHUNKS // 2) as pair:
                iteration(2 * pair, 0)
                iteration(2 * pair + 1, 1)
            for i in range(CHUNKS, LAST + 1):
                iteration(i, i % 2)

        block = ctx.enter_context(nc.Block())

        @block.sync
        def _(sp):
            for n in range(SLOTS):
                sp.dma_start(stage[:, n, :, :], w_stage[n]).then_inc(piece_in[n], 16)
            for n in range(SLOTS, 2 * SLOTS):
                if n - SLOTS < 3:
                    sp.wait_ge(cond_prod_done, n - SLOTS + 1)
                else:
                    sp.wait_ge(split_done, 1)
                sp.dma_start(stage[:, n % SLOTS, :, :], w_stage[n]).then_inc(piece_in[n % SLOTS], 16)

            def load_w2(p, slot):
                sp.dma_start(stage[:, slot, :, :].rearrange("p k n -> p (k n)"), w2_in[bass.ds(p, 1), :, :].rearrange("a p n -> p (a n)")).then_inc(piece_in[slot], 16)

            sp.dma_start(X[:, 1, :, :], x_in[1]).then_inc(x_loaded[1], 16)
            for p in range(SLOTS):
                if p < 3:
                    sp.wait_ge(split_done, p + 2)
                else:
                    sp.wait_ge(h_prod_done, 1)
                load_w2(p, p)
            with sp.Fori(1, 4) as q:
                for j in range(SLOTS):
                    sp.wait_ge(w2_done, 4 * q + j - 3)
                    load_w2(4 * q + j, j)
            sp.wait_ge(x1_added, STEPS + 1)
            sp.dma_start(X[:, 0, :, :], x_in[2]).then_inc(x_loaded[0], 16)
            with sp.Fori(4, 8) as q:
                for j in range(SLOTS):
                    sp.wait_ge(w2_done, 4 * q + j - 3)
                    load_w2(4 * q + j, j)

            def iteration(i, par):
                if on(i, 2, CHUNKS - 2):
                    sp.wait_ge(x1_added, STEPS * i + 1)
                    load_x(i + 1, 1 - par)
                if l3_on(i):
                    sp.wait_ge(out_ready, i - 2)
                    sp.dma_start(chunk_of(out, i - 3), OUTB[:, :, :].rearrange("p k n -> p (k n)")).then_inc(stored, 16)

            def chunk_of(t, c):
                if isinstance(c, int):
                    return t[c].rearrange("p k n -> p (k n)")
                return t[bass.ds(c, 1), :, :, :].rearrange("a p k n -> p (a k n)")

            def load_x(c, par):
                sp.dma_start(X[:, par, :, :].rearrange("p k n -> p (k n)"), chunk_of(x_in, c)).then_inc(x_loaded[par], 16)

            for i in range(HEAD):
                iteration(i, i % 2)
            with sp.Fori(HEAD // 2, CHUNKS // 2 - 1) as pair:
                iteration(2 * pair, 0)
                iteration(2 * pair + 1, 1)
            for i in range(CHUNKS - 2, LAST + 1):
                iteration(i, i % 2)
            sp.wait_ge(stored, 16 * CHUNKS)

        @block.gpsimd
        def _(pool):
            pool.memset(identf[:, :], 0.0).then_inc(ident_set, 1)
            pool.memset(identb[:, :], 0.0).then_inc(ident_set, 1)
            pool.wait_ge(ident_set, 2)
            for m in (identf, identb):
                pool.affine_select(out=m[:, :], in_=m[:, :], compare_op=ALU.not_equal, fill=1.0, base=0,
                                   pattern=[[-1, P]], channel_multiplier=1).then_inc(idents, 1)
            pool.memset(X1[:, 0, :, 0:HIST], 0.0).then_inc(x1_added, 1)
            pool.memset(zeros[:, :], 0.0).then_inc(x3_added, 1)

            def step(i, par, t, khalf, tap):
                step0, step2 = STEPS * i + t, STEPS * (i - 2) + t
                if conv_on(i):
                    ks = slice(2 * khalf, 2 * khalf + 2)
                    weight = condT[:, ks, bass.ds(tap, 1)].to_broadcast([P, 2, TOK])
                    done = STEPS * (i - 1) + t
                    pool.wait_ge(conv_added, done + i)
                    pool.tensor_tensor(CM[:, :, :], X1[:, 1 - par, ks, bass.ds(tap * B, TOK)], weight,
                                       ALU.mult).then_inc(conv_mul, 1)
                    pool.wait_ge(conv_mul, done + 1)
                    pool.tensor_tensor(CONV[:, ks, :], CONV[:, ks, :], CM[:, :, :], ALU.add).then_inc(conv_added, 1)
                if l2_on(i):
                    pool.wait_ge(hg_ready, step2 + 2)
                    pool.tensor_tensor(X3[:, :, bass.ds(t * B, B)], X2[:, :, bass.ds(t * B, B)], HG[:, 0, :, :],
                                       ALU.add).then_inc(x3_added, 1)
                if l0_on(i):
                    pool.wait_ge(h_ready[0], step0 + 2)
                    pool.wait_ge(h_ready[1], step0 + 2)
                    pool.tensor_tensor(X1[:, par, :, bass.ds(t * B + HIST, B)], X[:, par, :, bass.ds(t * B, B)],
                                       HS[:, 0, :, :], ALU.add).then_inc(x1_added, 1)

            def iteration(i, par):
                if on(i, 1, CHUNKS + 1):
                    pool.wait_ge(x1_added, STEPS * l0_chunks(i - 1) + 1)
                if l2_on(i):
                    pool.wait_ge(x3_added, STEPS * (i - 2) + 1)
                    pool.tensor_tensor(X2[:, :, :], X1[:, par, :, HIST:HIST + TOK], over_tok(vec(V_BO)),
                                       ALU.add).then_inc(x2_init, 1)
                if conv_on(i):
                    if on(i, 2, LAST):
                        pool.tensor_copy(X1[:, 1 - par, :, 0:HIST], X1[:, par, :, TOK:TOK + HIST]).then_inc(hist_copied, 1)
                        pool.wait_ge(hist_copied, i - 1)
                    if on(i, 2, LAST):
                        pool.wait_ge(l1_proj_done, i - 1)
                    pool.tensor_tensor(CONV[:, :, :], over_tok(vec(V_CONVB)), over_tok(zeros[:, :]),
                                       ALU.add).then_inc(conv_added, 1)
                if l0_on(i) or l2_on(i):
                    if at(i, LAST):
                        return
                    for khalf in range(2):
                        with pool.Fori(0, TAPS) as tap:
                            step(i, par, TAPS * khalf + tap, khalf, tap)

            pool.wait_ge(vecs_loaded, 16)
            pool.wait_ge(x_loaded[0], 16)
            iteration(0, 0)
            pool.wait_ge(x_loaded[1], 16)
            for i in range(1, HEAD):
                iteration(i, i % 2)
            with pool.Fori(HEAD // 2, CHUNKS // 2) as pair:
                iteration(2 * pair, 0)
                iteration(2 * pair + 1, 1)
            for i in range(CHUNKS, CHUNKS + 2):
                iteration(i, i % 2)

        @block.scalar
        def _(act):
            act.dma_start(cond[:, :], cond_in).then_inc(cond_loaded, 16)
            act.dma_start(X[:, 0, :, :], x_in[0]).then_inc(x_loaded[0], 16)
            act.dma_start(vecs[:, :], vecs_in).then_inc(vecs_loaded, 16)
            act.dma_start(PW[:, 0, :, :], w_proj[0]).then_inc(w_proj_in[0], 16)
            act.dma_start(small[:, :], small_in).then_inc(small_loaded, 16)
            for n in range(1, 6):
                act.dma_start(PW[:, n, :, :], w_proj[n]).then_inc(w_proj_in[n], 16)
            for dst, src in ((WP, wp_in), (WS, ws_in)):
                act.dma_start(dst[:, :, :], src).then_inc(l1w_in, 16)
            act.dma_start(WO[:, :], wo_in).then_inc(l1w_in, 16)
            act.wait_ge(ln_var, 1)
            act.activation(lns[:, 0:1], lns[:, 3:4], ACT.Sqrt).then_inc(ln_root, 1)
            act.preload_act_table_set("sigmoid_and_others")
            act.wait_ge(pro_abs, 1)
            act.activation(sp2[:, 1, :], sp2[:, 0, :], ACT.Sigmoid).then_inc(pro_sig, 1)
            for n, g in enumerate((GR, GZ, GH)):
                slot = (3, 0, 1)[n]
                act.wait_ge(piece_in[slot], 16 if n == 0 else 32)
                for k in range(KT):
                    act.activation(U[:, g, 0, k, :], stage[:, slot, k, :], ACT.Copy).then_inc(hi_done, 1)
                for k in range(KT):
                    act.wait_ge(rem_done, KT * n + k + 1)
                    act.activation(U[:, g, 1, k, :], stage[:, slot, k, :], ACT.Copy).then_inc(mid_done3, 1)
            act.wait_ge(piece_in[2], 32)
            for k in range(KT):
                act.activation(U[:, GG, 0, k, :], stage[:, 2, k, :], ACT.Copy).then_inc(hi_done, 1)
            for k in range(KT):
                act.wait_ge(rem_done, KT * 3 + k + 1)
                act.activation(U[:, GG, 1, k, :], stage[:, 2, k, :], ACT.Copy).then_inc(mid_done3, 1)
            act.wait_ge(h_pre_ready, 1)
            act.activation(hT[:, :, :], hpre[:, :, :], ACT.Gelu).then_inc(ht_ready, 1)
            act.preload_act_table_set("sigmoid_and_others")

            def step(i, t, j8):
                now0 = act.snap(STEPS * i + t + 1) if l0_on(i) else None
                now2 = act.snap(STEPS * (i - 2) + t + 1) if l2_on(i) else None
                if l2_on(i):
                    act.activation(ZX[:, :, :], X2[:, :, bass.ds(t * B, B)], ACT.Copy).then_inc(zx_copied, 1)
                    act.wait_ge(sumG_done, now2)
                    act.activation(GT[:, :, :], SG[:, :, :], ACT.Sigmoid).then_inc(gate_ready, 1)
                    act.wait_ge(gp_ready, now2)
                    act.wait_ge(x3_added, now2)
                    act.activation(HG[:, 0, :, :], GP[:, :, :], ACT.Tanh).then_inc(hg_new, 1)
                if l0_on(i):
                    for j, ks in HALVES:
                        act.wait_ge(sumR_done[j], now0)
                        act.activation(RT[:, ks, :], SR[:, ks, :], ACT.Sigmoid).then_inc(r_ready[j], 1)
                    act.wait_ge(sumZ_done, now0)
                    act.activation(ZT[:, :, :], SZ[:, :, :], ACT.Sigmoid).then_inc(z_ready, 1)
                    if w2_on(i):
                        act.wait_ge(w2_done, now0)
                        act.activation(w2rows[:, :], (C0, C1)[j8 % 2][0:B, :], ACT.Copy).then_inc(w2_rows_copied, 1)
                    for j, ks in HALVES:
                        act.wait_ge(sumH_done[j], now0)
                        act.activation(HT[:, ks, :], SH[:, ks, :], ACT.Tanh).then_inc(hh_ready[j], 1)

            def iteration(i, par):
                if l2_on(i):
                    act.wait_ge(l1_abs, i - 1)
                    act.activation(QS[:, :], AX1[:, :], ACT.Sigmoid).then_inc(l1_sig, 1)
                    act.wait_ge(l1_c, i - 1)
                    act.activation(CT[:, :], CL[:, :], ACT.Tanh).then_inc(l1_tanh, 1)
                if l3_on(i):
                    act.wait_ge(mid_done, i - 2)
                    act.activation(MT[:, :, :].rearrange("p k n -> p (k n)"), C2[:, :], ACT.Gelu).then_inc(mid_act, 1)
                    act.preload_act_table_set("sigmoid_and_others")
                if at(i, LAST):
                    return
                if l2_on(i):
                    act.wait_ge(x2_ready, i - 1)
                with act.Fori(0, STEPS // 8) as q:
                    for j in range(8):
                        step(i, 8 * q + j, j)

            wavefront(act, iteration)

        @block.vector
        def _(dve):
            dve.memset(HS[:, :, 0:2, :], 0.0).then_inc(h_ready[0], 1)
            dve.memset(HS[:, :, 2:4, :], 0.0).then_inc(h_ready[1], 1)
            dve.memset(YS[:, :, :], 0.0).then_inc(lr_evac, 1)
            dve.memset(decmask[:, :, :], 1.0).then_inc(lr_evac, 1)
            pro = Count(0)
            dve.wait_ge(lr_evac, 2)
            dve.memset(decmask[:, :, 0:1], 0.0).then_inc(pro_chain, 1)
            dve.wait_ge(pro_chain, pro.next())

            dve.wait_ge(cond_loaded, 16)
            dve.tensor_reduce(lns[:, 0:1], cond[:, :], AX.X, ALU.add).then_inc(pro_chain, 1)
            dve.wait_ge(pro_chain, pro.next())
            dve.tensor_scalar(lns[:, 1:2], lns[:, 0:1], 1.0 / E, None, ALU.mult).then_inc(pro_chain, 1)
            dve.wait_ge(pro_chain, pro.next())
            dve.tensor_scalar(cond[:, :], cond[:, :], lns[:, 1:2], None, ALU.subtract).then_inc(pro_chain, 1)
            dve.wait_ge(pro_chain, pro.next())
            dve.tensor_tensor(lnsq[:, :], cond[:, :], cond[:, :], ALU.mult).then_inc(pro_chain, 1)
            dve.wait_ge(pro_chain, pro.next())
            dve.tensor_reduce(lns[:, 2:3], lnsq[:, :], AX.X, ALU.add).then_inc(pro_chain, 1)
            dve.wait_ge(pro_chain, pro.next())
            dve.tensor_scalar(lns[:, 3:4], lns[:, 2:3], 1.0 / E, LN_EPS, ALU.mult, ALU.add).then_inc(ln_var, 1)
            dve.wait_ge(ln_root, 1)
            dve.reciprocal(lns[:, 1:2], lns[:, 0:1]).then_inc(pro_chain, 1)
            dve.wait_ge(pro_chain, pro.next())
            dve.scalar_tensor_tensor(lns[:, 2:3], lns[:, 3:4], lns[:, 1:2], lns[:, 0:1], ALU.mult, ALU.add).then_inc(pro_chain, 1)
            dve.wait_ge(pro_chain, pro.next())
            dve.tensor_scalar(lns[:, 2:3], lns[:, 2:3], 0.5, None, ALU.mult).then_inc(pro_chain, 1)
            dve.wait_ge(pro_chain, pro.next())
            dve.reciprocal(lns[:, 0:1], lns[:, 2:3]).then_inc(pro_chain, 1)
            dve.wait_ge(pro_chain, pro.next())
            dve.tensor_scalar(cn[:, :], cond[:, :], lns[:, 0:1], None, ALU.mult).then_inc(ln_ready, 1)
            def softplus(chain, ch, q, relu, d, r, sv, w, a, res):
                dve.tensor_scalar(d, q, -1.0, 2.0, ALU.mult, ALU.add).then_inc(chain, 1)
                dve.wait_ge(chain, ch.next())
                dve.reciprocal(r, d).then_inc(chain, 1)
                dve.wait_ge(chain, ch.next())
                dve.tensor_tensor(sv, q, r, ALU.mult).then_inc(chain, 1)
                dve.wait_ge(chain, ch.next())
                dve.tensor_tensor(w, sv, sv, ALU.mult).then_inc(chain, 1)
                dve.wait_ge(chain, ch.next())
                dve.tensor_scalar(a, w, 1.0 / (2 * SERIES + 1), None, ALU.mult).then_inc(chain, 1)
                dve.wait_ge(chain, ch.next())
                for n in range(SERIES - 1, 0, -1):
                    dve.scalar_tensor_tensor(a, a, 1.0 / (2 * n + 1), w, ALU.add, ALU.mult).then_inc(chain, 1)
                    dve.wait_ge(chain, ch.next())
                dve.scalar_tensor_tensor(a, a, 1.0, sv, ALU.add, ALU.mult).then_inc(chain, 1)
                dve.wait_ge(chain, ch.next())
                dve.scalar_tensor_tensor(res, a, 2.0, relu, ALU.mult, ALU.add).then_inc(chain, 1)
                dve.wait_ge(chain, ch.next())

            dve.wait_ge(small_loaded, 16)
            dve.tensor_scalar(sp2[:, 2, :], small[:, S_ALOG:S_ALOG + 2], 0.0, None, ALU.max).then_inc(pro_chain, 1)
            dve.wait_ge(pro_chain, pro.next())
            dve.scalar_tensor_tensor(sp2[:, 0, :], sp2[:, 2, :], -2.0, small[:, S_ALOG:S_ALOG + 2], ALU.mult, ALU.add).then_inc(pro_abs, 1)
            dve.wait_ge(pro_sig, 1)
            softplus(pro_chain, pro, sp2[:, 1, :], sp2[:, 2, :], sp2[:, 3, :], sp2[:, 4, :], sp2[:, 5, :], sp2[:, 0, :],
                     sp2[:, 3, :], sp2[:, 4, :])
            dve.tensor_copy(dec_dt[:, 1:2], sp2[:, 4, 1:2]).then_inc(pro_chain, 1)
            dve.wait_ge(pro_chain, pro.next())
            dve.scalar_tensor_tensor(dec_dt[:, 0:1], sp2[:, 4, 0:1], -1.0, sp2[:, 4, 1:2], ALU.mult, ALU.mult).then_inc(pro_chain, 1)
            dve.wait_ge(pro_chain, pro.next())
            dve.tensor_scalar(dec_dt[:, 0:1], dec_dt[:, 0:1], 1.0, None, ALU.add).then_inc(pro_chain, 1)
            dve.wait_ge(pro_chain, pro.next())
            dve.tensor_scalar(decmask[:, :, :], decmask[:, :, :], dec_dt[:, 0:1], None, ALU.mult).then_inc(pro_chain, 1)
            dve.wait_ge(pro_chain, pro.next())
            dve.wait_ge(vecs_loaded, 16)
            dve.tensor_copy(HG[:, 0, :, :], condT).then_inc(pro_chain, 1)
            dve.wait_ge(pro_chain, pro.next())
            dve.tensor_tensor(HG[:, 1, :, :], HG[:, 0, :, :], HGh[:, 0, :, :, 1], ALU.subtract).then_inc(pro_chain, 1)
            dve.wait_ge(pro_chain, pro.next())
            dve.tensor_tensor(HG[:, 2, :, :], HG[:, 1, :, :], HGh[:, 1, :, :, 1], ALU.subtract).then_inc(hg_ready, 1)
            dve.tensor_scalar(leak[:, :], vec(V_ALPHA), -1.0, 1.0, ALU.mult, ALU.add).then_inc(pro_chain, 1)
            dve.wait_ge(pro_chain, pro.next())
            dve.wait_ge(idents, 2)
            dve.tensor_reduce(batchmask[:, :], identf[0:LR, 0:LR].rearrange("p (r b) -> p b r", b=B), AX.X, ALU.add).then_inc(pro_chain, 1)
            dve.wait_ge(pro_chain, pro.next())
            dve.wait_ge(ct_prod_done, 1)
            dve.tensor_tensor(cTg[:, :, :], C2[:, 0:KT * B].rearrange("p (k b) -> p k b", b=B),
                              over_b(vec(V_GAMMA)), ALU.mult).then_inc(pro_chain, 1)
            dve.wait_ge(pro_chain, pro.next())
            dve.tensor_tensor(cT[:, :, :], cTg[:, :, :], over_b(vec(V_BETA)), ALU.add).then_inc(ct_ready, 1)
            def split_weights(n, g, slot):
                for k in range(KT):
                    dve.wait_ge(hi_done, KT * n + k + 1)
                    dve.tensor_tensor(stage[:, slot, k, :], stage[:, slot, k, :], U[:, g, 0, k, :], ALU.subtract).then_inc(rem_done, 1)
                for k in range(KT):
                    dve.wait_ge(mid_done3, KT * n + k + 1)
                    last = dve.tensor_tensor(U[:, g, 2, k, :], stage[:, slot, k, :], U[:, g, 1, k, :], ALU.subtract)
                last.then_inc(split_done, 1)

            split_weights(0, GR, 3)
            for g, v in ((GR, V_BR), (GZ, V_BZ), (GH, V_B)):
                dve.wait_ge(cond_prod_done, g + 1)
                bankg = (C0, C1, C3)[g]
                dve.tensor_tensor(vbias[:, g, :, :], bankg[:, 0:KT * B].rearrange("p (k b) -> p k b", b=B),
                                  over_b(vec(v)), ALU.add).then_inc(vb_ready, 1)
            split_weights(1, GZ, 0)
            split_weights(2, GH, 1)
            split_weights(3, GG, 2)
            dve.wait_ge(h_prod_done, 1)
            dve.tensor_tensor(hpre[:, :, :], C2[:, 64:64 + KT * B].rearrange("p (k b) -> p k b", b=B),
                              over_b(vec(V_BIAS1)), ALU.add).then_inc(h_pre_ready, 1)

            def reduce_parts(dst, src, n):
                return dve.tensor_reduce(dst, src[:, 0:n * PARTS * B].rearrange("p (m g b) -> p m b g", g=PARTS, b=B), AX.X, ALU.add)


            def reset_h(j, now0):
                ks = HALVES[j][1]
                dve.wait_ge(r_ready[j], now0)
                dve.tensor_tensor(RH[:, 0, ks, :], RT[:, ks, :], HS[:, 0, ks, :], ALU.mult).then_inc(rh_new[j], 1)

            def reset_h_remainder(j, now0):
                ks = HALVES[j][1]
                dve.wait_ge(rh_new[j], now0)
                dve.tensor_tensor(RH[:, 1, ks, :], RH[:, 0, ks, :], RHh[:, 0, ks, :, 1], ALU.subtract).then_inc(rh_rem[j], 1)

            def reset_h_last(j, now0):
                ks = HALVES[j][1]
                dve.wait_ge(rh_rem[j], now0)
                dve.tensor_tensor(RH[:, 2, ks, :], RH[:, 1, ks, :], RHh[:, 1, ks, :, 1], ALU.subtract).then_inc(rh_ready[j], 1)

            def z_candidate(j, now0):
                ks = HALVES[j][1]
                dve.wait_ge(hh_ready[j], now0)
                dve.tensor_tensor(ZH[:, ks, :], ZT[:, ks, :], HT[:, ks, :], ALU.mult).then_inc(zh_done[j], 1)

            def next_h(j, now0):
                ks = HALVES[j][1]
                dve.wait_ge(zh_done[j], now0)
                dve.tensor_tensor(HS[:, 0, ks, :], ZH[:, ks, :], ZC[:, ks, :], ALU.subtract).then_inc(h_new[j], 1)

            def next_h_remainder(j, now0):
                ks = HALVES[j][1]
                dve.wait_ge(h_new[j], now0)
                dve.tensor_tensor(HS[:, 1, ks, :], HS[:, 0, ks, :], HSh[:, 0, ks, :, 1], ALU.subtract).then_inc(h_rem[j], 1)

            def next_h_last(j, now0):
                ks = HALVES[j][1]
                dve.wait_ge(h_rem[j], now0)
                dve.tensor_tensor(HS[:, 2, ks, :], HS[:, 1, ks, :], HSh[:, 1, ks, :, 1], ALU.subtract).then_inc(h_ready[j], 1)

            def step(i, t):
                now0 = dve.snap(STEPS * i + t + 1) if l0_on(i) else None
                now2 = dve.snap(STEPS * (i - 2) + t + 1) if l2_on(i) else None
                if l2_on(i):
                    dve.wait_ge(preG_done, now2)
                    dve.wait_ge(zx_copied, now2)
                    reduce_parts(SG[:, :, :], G, KT).then_inc(sumG_done, 1)
                    dve.tensor_tensor(HL[:, :, :], HG[:, 0, :, :], over_b(leak[:, :]), ALU.mult).then_inc(hl_done, 1)
                    dve.wait_ge(gate_ready, now2)
                    dve.wait_ge(hl_done, now2)
                    dve.tensor_tensor(GX[:, :, :], GT[:, :, :], ZX[:, :, :], ALU.mult).then_inc(gx_done, 1)
                    dve.wait_ge(gx_done, now2)
                    dve.tensor_tensor(GP[:, :, :], GX[:, :, :], HL[:, :, :], ALU.add).then_inc(gp_ready, 1)
                if l0_on(i):
                    for j, ks in HALVES:
                        dve.wait_ge(preR_done[j], now0)
                        reduce_parts(SR[:, ks, :], A[j], 2).then_inc(sumR_done[j], 1)
                    reset_h(0, now0)
                    reset_h_remainder(0, now0)
                    reset_h(1, now0)
                    reset_h_last(0, now0)
                    reset_h_remainder(1, now0)
                    reset_h_last(1, now0)
                if l2_on(i):
                    dve.wait_ge(hg_new, now2)
                    dve.tensor_tensor(HG[:, 1, :, :], HG[:, 0, :, :], HGh[:, 0, :, :, 1], ALU.subtract).then_inc(hg_rem, 1)
                    dve.wait_ge(hg_rem, now2)
                    dve.tensor_tensor(HG[:, 2, :, :], HG[:, 1, :, :], HGh[:, 1, :, :, 1], ALU.subtract).then_inc(hg_ready, 1)
                if l0_on(i):
                    dve.wait_ge(preZ_done, now0)
                    reduce_parts(SZ[:, :, :], Z, KT).then_inc(sumZ_done, 1)
                    dve.wait_ge(z_ready, now0)
                    dve.scalar_tensor_tensor(ZC[:, :, :], ZT[:, :, :], 1.0, HS[:, 0, :, :], ALU.subtract, ALU.mult).then_inc(zc_done, 1)
                    for j, ks in HALVES:
                        dve.wait_ge(preH_done[j], now0)
                        if j == 0:
                            dve.wait_ge(x1_added, now0)
                            dve.wait_ge(zc_done, now0)
                        reduce_parts(SH[:, ks, :], A[j], 2).then_inc(sumH_done[j], 1)
                    z_candidate(0, now0)
                    next_h(0, now0)
                    z_candidate(1, now0)
                    next_h_remainder(0, now0)
                    next_h(1, now0)
                    next_h_last(0, now0)
                    next_h_remainder(1, now0)
                    next_h_last(1, now0)
                if w2_on(i):
                    piece = STEPS * i + t
                    dve.wait_ge(w2_turned, now0)
                    dve.tensor_tensor(lowrank[:, bass.ds(piece, 1), :, :].rearrange("p a k b -> p (a k) b"),
                                      C2[:, 0:KT * B].rearrange("p (k b) -> p k b", b=B),
                                      vecs[:, bass.ds(piece * KT + V_BIAS2, KT)].unsqueeze(2).to_broadcast([P, KT, B]),
                                      ALU.add).then_inc(lr_evac, 1)

            def split_inputs(g, psum, bias, chain, base, ready):
                dve.tensor_tensor(F[:, g, 0, :, :].rearrange("p m (t b) -> p m t b", b=B),
                                  psum[:, :].rearrange("p (m t b) -> p m t b", m=KT, b=B), bias, ALU.add).then_inc(chain, 1)
                dve.wait_ge(chain, base + 1)
                dve.tensor_tensor(F[:, g, 1, :, :], F[:, g, 0, :, :], Fh[:, g, 0, :, :, 1], ALU.subtract).then_inc(chain, 1)
                dve.wait_ge(chain, base + 2)
                dve.tensor_tensor(F[:, g, 2, :, :], F[:, g, 1, :, :], Fh[:, g, 1, :, :, 1], ALU.subtract).then_inc(ready, 1)

            def vb(g):
                return vbias[:, g, :, :].unsqueeze(2).to_broadcast([P, KT, STEPS, B])

            def iteration(i, par):
                if at(i, 2):
                    dve.wait_ge(lr_evac, PIECES + 2)
                    for n, dst in ((1, B1[:, :, :, :]), (2, A2[:, :, :, :]), (0, A1B2[:, 0, :, :, :]), (3, A1B2[:, 1, :, :, :])):
                        dve.tensor_copy(dst, lowrank[:, n * RANK:(n + 1) * RANK, :, :].rearrange("p r k b -> p k r b")).then_inc(lr_packed, 1)
                if l3_on(i):
                    dve.wait_ge(lr_u_done, i - 2)
                    dve.tensor_tensor(UM[:, :].rearrange("p (t b) -> p t b", b=B), C2[0:LR, 0:TOK].rearrange("p (t b) -> p t b", b=B),
                                      mask_tok(), ALU.mult).then_inc(u_masked, 1)
                if l2_on(i):
                    dve.wait_ge(l1_proj_done, i - 1)
                    ch = Count(K_L1 * (i - 2))
                    dve.tensor_scalar(XB[:, :], C3[0:N1, 0:TOK], small[:, S_BPB:S_BPB + 1], None, ALU.add).then_inc(chain_l1, 1)
                    dve.wait_ge(chain_l1, ch.next())
                    dve.tensor_scalar(RL[:, :], XB[:, :], 0.0, None, ALU.max).then_inc(chain_l1, 1)
                    dve.wait_ge(chain_l1, ch.next())
                    dve.scalar_tensor_tensor(AX1[:, :], RL[:, :], -2.0, XB[:, :], ALU.mult, ALU.add).then_inc(l1_abs, 1)
                    dve.tensor_scalar(CL[:, :], C3[0:N1, TOK:2 * TOK], small[:, S_BPC:S_BPC + 1], None, ALU.add).then_inc(l1_c, 1)
                    dve.tensor_scalar(US[:, :], C3[0:N1, 2 * TOK:3 * TOK], small[:, S_BS:S_BS + 1], None, ALU.add).then_inc(l1_evac, 1)
                    dve.wait_ge(l1_evac, i - 1)
                    dve.wait_ge(l1_sig, i - 1)
                    softplus(chain_l1, ch, QS[:, :], RL[:, :], DS[:, :], RD[:, :], SS[:, :], WW[:, :], AC[:, :], SP[:, :])
                    dve.scalar_tensor_tensor(VV[:, :, :].rearrange("p b t -> p t b"), SP[:, :].rearrange("p (t b) -> p t b", b=B),
                                             dec_dt[:, 1:2], US[:, :].rearrange("p (t b) -> p t b", b=B), ALU.mult, ALU.mult).then_inc(chain_l1, 1)
                    dve.wait_ge(chain_l1, ch.next())
                    dve.scalar_tensor_tensor(VV[:, :, 0], YS[:, :, STEPS - 1], dec_dt[:, 0:1], VV[:, :, 0], ALU.mult, ALU.add).then_inc(chain_l1, 1)
                    dve.wait_ge(chain_l1, ch.next())
                    dve.tensor_tensor_scan(YS[:, :, :].rearrange("p b t -> p (b t)"), decmask[:, :, :].rearrange("p b t -> p (b t)"),
                                           VV[:, :, :].rearrange("p b t -> p (b t)"), 0.0, ALU.mult, ALU.add).then_inc(chain_l1, 1)
                    dve.wait_ge(chain_l1, ch.next())
                    dve.wait_ge(l1_tanh, i - 1)
                    dve.tensor_tensor(YT[:, :].rearrange("p (t b) -> p t b", b=B), CT[:, :].rearrange("p (t b) -> p t b", b=B),
                                      YS[:, :, :].rearrange("p b t -> p t b"), ALU.mult).then_inc(y_ready, 1)
                    assert ch.n == K_L1
                if l0_on(i):
                    for n, (g, psum) in enumerate(((GR, C0), (GZ, C1))):
                        dve.wait_ge((projR_done, projZ_done)[n], i + 1)
                        split_inputs(g, psum, vb(g), chain_f, 3 * K_F * i + K_F * n, (F_R, F_Z)[n])
                if l0_on(i):
                    dve.wait_ge(projH_done, i + 1)
                    split_inputs(GH, C3, vb(GH), chain_f, 3 * K_F * i + 2 * K_F, F_H)
                if l2_on(i):
                    dve.wait_ge(wo_done, i - 1)
                    dve.wait_ge(x2_init, i - 1)
                    dve.tensor_tensor(X2[:, :, :].rearrange("p k n -> p (k n)"), C0[:, :], X2[:, :, :].rearrange("p k n -> p (k n)"),
                                      ALU.add).then_inc(x2_ready, 1)
                if l3_on(i):
                    dve.wait_ge(v_done, i - 2)
                    dve.tensor_tensor(VM[:, :].rearrange("p (t b) -> p t b", b=B), C1[0:LR, 0:TOK].rearrange("p (t b) -> p t b", b=B),
                                      mask_tok(), ALU.mult).then_inc(v_masked, 1)
                if l2_on(i):
                    dve.wait_ge(projG_done, i - 1)
                    split_inputs(GG, C0, over_tok(vec(V_L2B)).rearrange("p m (t b) -> p m t b", b=B), chain_fg, K_F * (i - 2), F_G)
                if l3_on(i):
                    dve.wait_ge(out_done, i - 2)
                    if on(i, 4, LAST):
                        dve.wait_ge(stored, 16 * (i - 3))
                    dve.scalar_tensor_tensor(OUTB[:, :, :].rearrange("p k n -> p (k n)"), X3[:, :, :].rearrange("p k n -> p (k n)"), 2.0,
                                             C2[:, :], ALU.mult, ALU.add).then_inc(out_ready, 1)
                if at(i, 2):
                    for n, dst in ((0, A1T), (1, B2T)):
                        dve.wait_ge(lrt_done, n + 1)
                        dve.tensor_copy(dst[:, :], (Z, G)[n][0:LR, :]).then_inc(lrt_evac, 1)
                if at(i, LAST):
                    return
                with dve.Fori(0, STEPS // 8) as q:
                    for j in range(8):
                        step(i, 8 * q + j)

            wavefront(dve, iteration)

        @block.tensor
        def _(pe):
            def project(dst, weights, moving, start=True, stop=True, tiles=range(KT)):
                for m in tiles:
                    for k in range(KT):
                        last = pe.matmul(dst(m), weights(k, m), moving(k), start=start and m == 0 and k == 0,
                                         stop=stop and k == KT - 1, skip_group_check=True)
                return last

            def tile(t, m):
                return t[:, m * P:(m + 1) * P]

            pe.wait_ge(idents, 2)
            pe.wait_ge(ln_ready, 1)
            for k in range(KT):
                last = pe.matmul(C2[:, k * B:(k + 1) * B], cn[:, k * P:(k + 1) * P], identf[0:B, 0:B], start=k == 0, stop=True,
                                 skip_group_check=True)
            last.then_inc(ct_prod_done, 1)
            pe.wait_ge(vecs_loaded, 16)
            for g in range(3):
                pe.wait_ge(piece_in[g], 16)
                bankg = (C0, C1, C3)[g]
                project(lambda m: bankg[:, m * B:(m + 1) * B], lambda k, m: tile(stage[:, g, k, :], m),
                        lambda k: condT[:, k, :]).then_inc(cond_prod_done, 1)
            def hidden():
                pe.wait_ge(ct_ready, 1)
                pe.wait_ge(piece_in[3], 32)
                project(lambda m: C2[:, 64 + m * B:64 + (m + 1) * B], lambda k, m: tile(stage[:, 3, k, :], m),
                        lambda k: cT[:, k, :], ).then_inc(h_prod_done, 1)

            def product(g, moving, banks, inject_t, ready=None, now=None, prepare=None):
                for kh in range(2):
                    if kh == 1 and ready is not None:
                        pe.wait_ge(ready, now)
                    for psum, ms, done in banks:
                        for m in ms:
                            for k in (2 * kh, 2 * kh + 1):
                                for u in range(PARTS):
                                    at_col = (m - ms[0]) * PARTS * B
                                    last = pe.matmul(psum[:, at_col:at_col + PARTS * B], U[:, g, u, k, m * P:(m + 1) * P],
                                                     moving[:, :, k, :, 1], start=m == ms[0] and k == 0 and u == 0,
                                                     stop=k == KT - 1 and u == PARTS - 1, skip_group_check=True)
                        if kh == 1:
                            last.then_inc(done, 1)
                    if kh == 0:
                        for psum, ms, done in banks:
                            rhs = Fh[:, g, :, ms[0]:ms[-1] + 1, bass.ds(inject_t * B, B), 1].rearrange("p g m b -> p m g b")
                            pe.matmul(psum[:, 0:len(ms) * PARTS * B], identb[:, :], rhs, start=False, stop=False,
                                      skip_group_check=True)
                        if prepare is not None:
                            prepare()

            halves_r = ((A[0], (0, 1), preR_done[0]), (A[1], (2, 3), preR_done[1]))
            halves_h = ((A[0], (0, 1), preH_done[0]), (A[1], (2, 3), preH_done[1]))
            whole_z, whole_g = ((Z, (0, 1, 2, 3), preZ_done),), ((G, (0, 1, 2, 3), preG_done),)

            def step(i, t, j4, quarter):
                now = [None]

                def snap_now():
                    now[0] = pe.snap(STEPS * i + t + 1)

                if l2_on(i):
                    pe.wait_ge(hg_ready, STEPS * (i - 2) + t + 1)
                    product(GG, HGh, whole_g, t, prepare=snap_now if l0_on(i) else None)
                elif l0_on(i):
                    snap_now()
                if l0_on(i):
                    pe.wait_ge(h_ready[0], now[0])
                    product(GR, HSh, halves_r, t, h_ready[1], now[0])
                    product(GZ, HSh, whole_z, t)
                    if w2_on(i):
                        pe.wait_ge(piece_in[j4], 16 * (4 * i + 3) + 16 * quarter)
                        for k in range(KT):
                            last = pe.matmul((C0, C1)[j4 % 2][0:B, :], hT[:, k, :], stage[:, j4, k, :],
                                             start=k == 0, stop=k == KT - 1, skip_group_check=True)
                        last.then_inc(w2_done, 1)
                    pe.wait_ge(rh_ready[0], now[0])
                    product(GH, RHh, halves_h, t, rh_ready[1], now[0])
                    if w2_on(i):
                        pe.wait_ge(w2_rows_copied, now[0])
                        pe.wait_ge(lr_evac, STEPS * i + t + 2)
                        for m in range(KT):
                            last = pe.matmul(C2[:, m * B:(m + 1) * B], w2rows[:, m * P:(m + 1) * P], identf[0:B, 0:B],
                                             start=m == 0, stop=True, skip_group_check=True)
                        last.then_inc(w2_turned, 1)

            def iteration(i, par):
                if at(i, 2):
                    pe.wait_ge(lr_packed, 4)
                    for n in range(2):
                        for k in range(KT):
                            last = pe.matmul((Z, G)[n][0:LR, k * P:(k + 1) * P], A1B2[:, n, k, :, :].rearrange("p r b -> p (r b)"),
                                             identf[:, :], start=k == 0, stop=True, skip_group_check=True)
                        last.then_inc(lrt_done, 1)
                if l2_on(i):
                    pe.wait_ge(conv_added, (STEPS + 1) * (i - 1))
                    if at(i, 2):
                        pe.wait_ge(l1w_in, 48)
                    pe.wait_ge(F_H, l0_chunks(i - 1))
                    for n in range(3):
                        for k in range(KT):
                            if n < 2:
                                lhsT, rhs = WP[:, k, n * N1:(n + 1) * N1], CONV[:, k, :]
                            else:
                                lhsT, rhs = WS[:, k, :], X1[:, par, k, HIST:HIST + TOK]
                            last = pe.matmul(C3[0:N1, n * TOK:(n + 1) * TOK], lhsT, rhs, start=n == 0 and k == 0, stop=k == KT - 1,
                                             skip_group_check=True)
                    last.then_inc(l1_proj_done, 1)
                if l3_on(i):
                    pe.wait_ge(x3_added, STEPS * (i - 2) + 1)
                    if on(i, 4, LAST):
                        pe.wait_ge(out_ready, i - 3)
                    for k in range(KT):
                        last = pe.matmul(C2[0:LR, 0:TOK], A2[:, k, :, :].rearrange("p r b -> p (r b)"), X3[:, k, :],
                                         start=k == 0, stop=k == KT - 1, skip_group_check=True)
                    last.then_inc(lr_u_done, 1)
                if l0_on(i):
                    pe.wait_ge(x_loaded[par], x_count(i, par))
                    if w2_on(i):
                        pe.wait_ge(w_proj_in[0], 16)
                        pe.wait_ge(lr_evac, STEPS * i + 2)
                        pe.wait_ge(vb_ready, 3)
                    if isinstance(i, int) and i in (2, 3):
                        pe.wait_ge(lr_evac, PIECES + 2)
                    if on(i, 3, LAST):
                        pe.wait_ge(F_G, i - 2)
                    project(lambda m: tile(C0, m), lambda k, m: tile(PW[:, W_R, k, :], m), lambda k: X[:, par, k, :]).then_inc(projR_done, 1)
                    if at(i, 0):
                        pe.wait_ge(w_proj_in[1], 16)
                    if on(i, 4, LAST):
                        pe.wait_ge(v_masked, i - 3)
                    project(lambda m: tile(C1, m), lambda k, m: tile(PW[:, W_Z, k, :], m), lambda k: X[:, par, k, :]).then_inc(projZ_done, 1)
                if l3_on(i):
                    if at(i, 3):
                        pe.wait_ge(w_proj_in[4], 16)
                        pe.wait_ge(lrt_evac, 2)
                    pe.wait_ge(u_masked, i - 2)
                    project(lambda m: tile(C2, m), lambda k, m: tile(PW[:, W_DOWN, k, :], m), lambda k: X3[:, k, :], stop=False)
                    for m in range(KT):
                        last = pe.matmul(tile(C2, m), B2T[:, m * P:(m + 1) * P], UM[:, :], start=False, stop=True, skip_group_check=True)
                    last.then_inc(mid_done, 1)
                if l0_on(i):
                    if at(i, 0):
                        pe.wait_ge(w_proj_in[2], 16)
                    if on(i, 2, LAST):
                        pe.wait_ge(l1_evac, i - 1)
                    project(lambda m: tile(C3, m), lambda k, m: tile(PW[:, W_H, k, :], m), lambda k: X[:, par, k, :]).then_inc(projH_done, 1)
                if l2_on(i):
                    pe.wait_ge(F_R, l0_chunks(i))
                    if on(i, 3, LAST):
                        pe.wait_ge(F_G, i - 2)
                    pe.wait_ge(y_ready, i - 1)
                    for m in range(KT):
                        last = pe.matmul(tile(C0, m), WO[:, m * P:(m + 1) * P], YT[:, :], start=m == 0, stop=True, skip_group_check=True)
                    last.then_inc(wo_done, 1)
                if l3_on(i):
                    pe.wait_ge(F_Z, l0_chunks(i))
                    pe.wait_ge(mid_act, i - 2)
                    for k in range(KT):
                        last = pe.matmul(C1[0:LR, 0:TOK], B1[:, k, :, :].rearrange("p r b -> p (r b)"), MT[:, k, :],
                                         start=k == 0, stop=k == KT - 1, skip_group_check=True)
                    last.then_inc(v_done, 1)
                    if at(i, 3):
                        pe.wait_ge(w_proj_in[5], 16)
                    project(lambda m: tile(C2, m), lambda k, m: tile(PW[:, W_UP, k, :], m), lambda k: MT[:, k, :], stop=False,
                            tiles=(0, 1))
                if l2_on(i):
                    if at(i, 2):
                        pe.wait_ge(w_proj_in[3], 16)
                    pe.wait_ge(x2_ready, i - 1)
                    project(lambda m: tile(C0, m), lambda k, m: tile(PW[:, W_G, k, :], m), lambda k: X2[:, k, :]).then_inc(projG_done, 1)
                if l3_on(i):
                    project(lambda m: tile(C2, m), lambda k, m: tile(PW[:, W_UP, k, :], m), lambda k: MT[:, k, :], stop=False,
                            tiles=(2, 3))
                if l3_on(i):
                    pe.wait_ge(v_masked, i - 2)
                    for m in range(KT):
                        if m == 0 and l0_on(i):
                            pe.wait_ge(F_R, i + 1)
                            pe.wait_ge(F_Z, i + 1)
                            pe.wait_ge(F_H, i + 1)
                        if m == KT - 1 and l2_on(i):
                            pe.wait_ge(F_G, i - 1)
                        last = pe.matmul(tile(C2, m), A1T[:, m * P:(m + 1) * P], VM[:, :], start=False, stop=True, skip_group_check=True)
                    last.then_inc(out_done, 1)
                if at(i, LAST):
                    return
                if at(i, 0):
                    hidden()
                    pe.wait_ge(split_done, 3)
                    pe.wait_ge(ht_ready, 1)
                if at(i, 2):
                    pe.wait_ge(split_done, 4)
                    pe.wait_ge(lrt_evac, 2)
                if l0_on(i) and not l3_on(i):
                    pe.wait_ge(F_R, i + 1)
                    pe.wait_ge(F_Z, i + 1)
                    pe.wait_ge(F_H, i + 1)
                if at(i, 2):
                    pe.wait_ge(F_G, 1)
                with pe.Fori(0, STEPS // 4) as q:
                    for j in range(4):
                        step(i, 4 * q + j, j, q)

            def x_count(i, par):
                return 8 * (i - par) + 16

            wavefront(pe, iteration)


_OUT = (CHUNKS, P, KT, TOK)


def kernel(**inputs):
    import numpy as _np
    import concourse.bacc as _bacc
    from concourse import mybir as _mybir
    from concourse.bass_utils import run_bass_kernel_spmd as _run

    a = {k: _np.asarray(v) for k, v in inputs.items()}

    def rows(w):
        return w.reshape(KT, P, -1).transpose(1, 0, 2)

    def column(v):
        return v.reshape(KT, P).T

    x = a["x"].reshape(B, CHUNKS, STEPS, KT, P).transpose(1, 4, 3, 2, 0).reshape(CHUNKS, P, KT, TOK)
    wh, wz = a["L2_cond_W"][:, :E].T, a["L2_cond_W"][:, E:].T
    staged = [a["L0_cond_C_r"], a["L0_cond_C_z"], a["L0_cond_C"], a["L0_cond_U_r"],
              a["L0_cond_U_z"], a["L0_cond_U"], wh, a["L3_cond_W1"]]
    proj = [a["L0_cond_W_r"], a["L0_cond_W_z"], a["L0_cond_W"], wz, a["L3_cond_base_down"], a["L3_cond_base_up"].T]
    w2 = a["L3_cond_W2"].reshape(KT, P, 4, E, RANK).transpose(2, 4, 1, 0, 3).reshape(PIECES, P, KT * E)
    bias2 = a["L3_cond_bias2"].reshape(4, KT, P, RANK).transpose(2, 0, 3, 1).reshape(P, PIECES * KT)
    vecs = _np.concatenate([column(a[n]) for n in (
        "L0_cond_b_z", "L0_cond_b_r", "L0_cond_b", "L1_cond_conv_b", "L1_cond_bo", "L2_cond_b", "L2_cond_alpha",
        "L3_cond_ln_gamma", "L3_cond_ln_beta", "L3_cond_bias1")] + [bias2, rows(a["cond_1024"].T).reshape(P, KT * B)], axis=1)
    small = _np.stack([a["L1_cond_bp"][:N1], a["L1_cond_bp"][N1:], a["L1_cond_bs"], a["L1_cond_A_log"],
                       a["L1_cond_dt_log"]], axis=1)
    laid = {"x_in": x, "w_stage": _np.stack([rows(w) for w in staged]), "w2_in": w2,
            "w_proj": _np.stack([rows(w) for w in proj]), "vecs_in": vecs, "cond_in": a["cond_1024"],
            "wp_in": rows(a["L1_cond_Wp"]), "ws_in": rows(a["L1_cond_Ws"]), "wo_in": a["L1_cond_Wo"], "small_in": small}

    nc = _bacc.Bacc("TRN2", target_bir_lowering=False, num_devices=1)
    arrays, args = {}, []
    for name, v in laid.items():
        v = _np.ascontiguousarray(v)
        arrays[name + "_dram"] = v
        args.append(nc.dram_tensor(name + "_dram", v.shape, _mybir.dt.from_np(v.dtype), kind="ExternalInput").ap())
    args.append(nc.dram_tensor("out_dram", _OUT, _mybir.dt.float32, kind="ExternalOutput").ap())
    four_layer_kernel(nc, *args)
    r = _run(nc, [arrays], core_ids=[0])
    got = r.results[0]["out_dram"].reshape(CHUNKS, P, KT, STEPS, B)
    return _np.ascontiguousarray(got.transpose(4, 0, 3, 2, 1).reshape(B, T, E))
```
